# Optimizing a Trainium2 kernel written in Bass

```python
import numpy as np
import jax
import jax.numpy as jnp

def _softmax(x, axis=-1):
    return jax.nn.softmax(x, axis=axis)

def _gelu(x):
    return jax.nn.gelu(x, approximate=True)

def _silu(x):
    return jax.nn.silu(x)

def _sigmoid(x):
    return jax.nn.sigmoid(x)

def _layernorm(x, axis=-1, eps=1e-05):
    m = jnp.mean(x, axis=axis, keepdims=True)
    v = jnp.var(x, axis=axis, keepdims=True)
    return (x - m) / jnp.sqrt(v + eps)

def _scatter_add(tgt, idx, src, axis=0):
    return tgt.at[idx].add(src)

def _segment_sum(src, seg, n):
    return jax.ops.segment_sum(src, seg, n)
kernel_name = 'mk_cond_seq_d1_seqx_r8_f0c980'

def setup_inputs(seed: int=0):
    np.random.seed(seed)
    _w = jnp.asarray

    def _rec_inputs():
        import jax
        import jax.numpy as jnp
        _rk = jax.random.key(seed)
        x = 7.22e-05 + 1 * jax.random.normal(jax.random.fold_in(_rk, 1), (128, 32, 256), jnp.float32)
        _lenS = 32 - jax.random.randint(jax.random.fold_in(_rk, 7), (128,), 0, max(1, 32 // 4) + 1, jnp.int32)
        _lenS2 = 32 - jax.random.randint(jax.random.fold_in(_rk, 8), (128,), 0, max(1, 32 // 4) + 1, jnp.int32)
        cond_2048 = 0.0061147 + 1.02565 * jax.random.normal(jax.random.fold_in(_rk, 11), (128, 256), jnp.float32)
        return (x, cond_2048)
    x, cond_2048 = _rec_inputs()

    def _L0_cond_setup():
        import jax, jax.numpy as jnp
        import numpy as np
        D_MODEL = 256
        N_HEADS = 16
        N_KV_HEADS = 4
        HEAD_DIM = D_MODEL // N_HEADS
        N_GROUPS = N_HEADS // N_KV_HEADS
        BLOCK_SIZE = 128
        WINDOW = 32
        GLOBAL_EVERY = 64
        LATENT = 64
        ROPE_THETA = 10000.0
        LN_EPS = 1e-05

        def _rope_tables(T, dtype):
            freqs = 1.0 / ROPE_THETA ** (jnp.arange(0, HEAD_DIM, 2, dtype=jnp.float32) / HEAD_DIM)
            emb = jnp.arange(T, dtype=jnp.float32)[:, None] * freqs[None, :]
            cos = jnp.concatenate([jnp.cos(emb), jnp.cos(emb)], axis=-1).astype(dtype)
            sin = jnp.concatenate([jnp.sin(emb), jnp.sin(emb)], axis=-1).astype(dtype)
            return (cos, sin)

        def _rotate_half(x):
            h = x.shape[-1] // 2
            return jnp.concatenate([-x[..., h:], x[..., :h]], axis=-1)

        def _sparse_mask(T):
            idx = jnp.arange(T)
            blk = idx // BLOCK_SIZE
            future_block = blk[None, :] > blk[:, None]
            outside_window = jnp.abs(idx[None, :] - idx[:, None]) > WINDOW
            global_visible = jnp.broadcast_to((idx % GLOBAL_EVERY == 0)[None, :], (T, T))
            return outside_window & ~global_visible | future_block
        key = jax.random.key(seed)
        ks = jax.random.split(key, 9)
        B, T = (2, 256)
        s = 0.02
        return {'x': jax.random.normal(ks[0], (B, T, D_MODEL), jnp.float32), 't_emb': jax.random.normal(ks[1], (B, D_MODEL), jnp.float32), 'W_ada': jax.random.normal(ks[2], (2 * D_MODEL, D_MODEL), jnp.float32) * s, 'b_ada': jnp.zeros((2 * D_MODEL,), jnp.float32), 'Wq': jax.random.normal(ks[3], (N_HEADS * HEAD_DIM, D_MODEL), jnp.float32) * s, 'Wkd': jax.random.normal(ks[4], (LATENT, D_MODEL), jnp.float32) * s, 'Wku': jax.random.normal(ks[5], (N_KV_HEADS * HEAD_DIM, LATENT), jnp.float32) * s, 'Wvu': jax.random.normal(ks[6], (N_KV_HEADS * HEAD_DIM, LATENT), jnp.float32) * s, 'Wo': jax.random.normal(ks[7], (D_MODEL, N_HEADS * HEAD_DIM), jnp.float32) * s}
    _L0_cond_all = _L0_cond_setup()
    _L0_cond_in = {k: v for k, v in _L0_cond_all.items() if k in ('W_ada', 'b_ada', 'Wq', 'Wkd', 'Wku', 'Wvu', 'Wo')}
    del _L0_cond_all
    return {'x': x, 'cond_2048': cond_2048, 'L0_cond_W_ada': _L0_cond_in['W_ada'], 'L0_cond_b_ada': _L0_cond_in['b_ada'], 'L0_cond_Wq': _L0_cond_in['Wq'], 'L0_cond_Wkd': _L0_cond_in['Wkd'], 'L0_cond_Wku': _L0_cond_in['Wku'], 'L0_cond_Wvu': _L0_cond_in['Wvu'], 'L0_cond_Wo': _L0_cond_in['Wo']}

def reference(x, cond_2048, L0_cond_W_ada, L0_cond_b_ada, L0_cond_Wq, L0_cond_Wkd, L0_cond_Wku, L0_cond_Wvu, L0_cond_Wo):
    import jax
    import jax.numpy as jnp

    def _L0_cond_ref(x, t_emb, W_ada, b_ada, Wq, Wkd, Wku, Wvu, Wo):
        import jax, jax.numpy as jnp
        import numpy as np
        D_MODEL = 256
        N_HEADS = 16
        N_KV_HEADS = 4
        HEAD_DIM = D_MODEL // N_HEADS
        N_GROUPS = N_HEADS // N_KV_HEADS
        BLOCK_SIZE = 128
        WINDOW = 32
        GLOBAL_EVERY = 64
        LATENT = 64
        ROPE_THETA = 10000.0
        LN_EPS = 1e-05

        def _rope_tables(T, dtype):
            freqs = 1.0 / ROPE_THETA ** (jnp.arange(0, HEAD_DIM, 2, dtype=jnp.float32) / HEAD_DIM)
            emb = jnp.arange(T, dtype=jnp.float32)[:, None] * freqs[None, :]
            cos = jnp.concatenate([jnp.cos(emb), jnp.cos(emb)], axis=-1).astype(dtype)
            sin = jnp.concatenate([jnp.sin(emb), jnp.sin(emb)], axis=-1).astype(dtype)
            return (cos, sin)

        def _rotate_half(x):
            h = x.shape[-1] // 2
            return jnp.concatenate([-x[..., h:], x[..., :h]], axis=-1)

        def _sparse_mask(T):
            idx = jnp.arange(T)
            blk = idx // BLOCK_SIZE
            future_block = blk[None, :] > blk[:, None]
            outside_window = jnp.abs(idx[None, :] - idx[:, None]) > WINDOW
            global_visible = jnp.broadcast_to((idx % GLOBAL_EVERY == 0)[None, :], (T, T))
            return outside_window & ~global_visible | future_block
        B, T, C = x.shape
        proj = t_emb @ W_ada.T + b_ada
        scale, shift = (proj[:, :C], proj[:, C:])
        mu = jnp.mean(x, axis=-1, keepdims=True)
        var = jnp.mean(jnp.square(x - mu), axis=-1, keepdims=True)
        h = (x - mu) * jax.lax.rsqrt(var + LN_EPS)
        h = h * (1.0 + scale[:, None, :]) + shift[:, None, :]
        q = (h @ Wq.T).reshape(B, T, N_HEADS, HEAD_DIM).transpose(0, 2, 1, 3)
        c_kv = h @ Wkd.T
        k = (c_kv @ Wku.T).reshape(B, T, N_KV_HEADS, HEAD_DIM).transpose(0, 2, 1, 3)
        v = (c_kv @ Wvu.T).reshape(B, T, N_KV_HEADS, HEAD_DIM).transpose(0, 2, 1, 3)
        cos, sin = _rope_tables(T, x.dtype)
        cos, sin = (cos[None, None], sin[None, None])
        q = q * cos + _rotate_half(q) * sin
        k = k * cos + _rotate_half(k) * sin
        k_exp = jnp.repeat(k, N_GROUPS, axis=1)
        v_exp = jnp.repeat(v, N_GROUPS, axis=1)
        mask = _sparse_mask(T)
        scores = jnp.einsum('bhtd,bhsd->bhts', q, k_exp) / jnp.sqrt(jnp.asarray(HEAD_DIM, x.dtype))
        scores = jnp.where(mask[None, None], jnp.asarray(-jnp.inf, x.dtype), scores)
        attn = jax.nn.softmax(scores, axis=-1)
        y = jnp.einsum('bhts,bhsd->bhtd', attn, v_exp)
        out = y.transpose(0, 2, 1, 3).reshape(B, T, C) @ Wo.T
        return x + out
    x = _L0_cond_ref(x, cond_2048, L0_cond_W_ada, L0_cond_b_ada, L0_cond_Wq, L0_cond_Wkd, L0_cond_Wku, L0_cond_Wvu, L0_cond_Wo)
    return x

_drawn_inputs = setup_inputs


def setup_inputs(seed=0):
    import zlib

    import numpy as np

    out = dict(_drawn_inputs(seed))
    spreads = {'L0_cond_b_ada': (0.0, 0.8)}
    factors = {'cond_2048': 8.0,
     'L0_cond_W_ada': 8.0,
     'L0_cond_Wq': 8.0,
     'L0_cond_Wkd': 8.0,
     'L0_cond_Wku': 8.0,
     'L0_cond_Wvu': 8.0,
     'L0_cond_Wo': 8.0}
    for name, (base, spread) in spreads.items():
        noise = np.random.default_rng([zlib.crc32(name.encode()), seed]).standard_normal(out[name].shape)
        drawn = base * np.exp(spread * noise) if base else spread * noise
        out[name] = jnp.asarray(drawn.astype(out[name].dtype))
    for name, factor in factors.items():
        out[name] = (out[name] * factor).astype(out[name].dtype)
    return out
```

```python
from contextlib import ExitStack

import numpy as np

import concourse.bass as bass
from concourse import mybir

F32 = mybir.dt.float32
ALU = mybir.AluOpType
ACT = mybir.ActivationFunctionType
AX = mybir.AxisListType

P = 128
B, T, D = 128, 32, 256
HQ, G, HD = 16, 4, 16
J = HQ // G
HALF = HD // 2
LATENT = 64
EPS = 1e-5
THETA = 10000.0
SCALE = float(HD) ** -0.5
BU = P // T
UNITS = B * T // P
KT = D // P
GD = G * HD
DQ = HQ * HD
LOAD_AHEAD = 8

NORM, STATS, TR, QKV, ATT, PRB, OUT = 3, 4, 2, 1, 0, -1, -2
FIRST_FULL = 4
LAST_FULL = UNITS - STATS
FIRST, LAST = -STATS, UNITS + 2


def rope_tables():
    freqs = (1.0 / np.float32(THETA) ** (np.arange(0, HD, 2, dtype=np.float32) / np.float32(HD))).astype(np.float32)
    emb = np.arange(T, dtype=np.float32)[:, None] * freqs[None, :]
    cos, sin = np.cos(emb).astype(np.float32), np.sin(emb).astype(np.float32)
    spread = lambda first, second: np.stack([first, second], 1)[:, :, None, :].repeat(G, 2).reshape(T, GD)
    plain = np.stack([spread(cos, cos), spread(sin, sin)], 1)
    swap = np.stack([spread(-sin, sin), spread(cos, -cos)], 1)
    return np.tile(np.stack([plain, swap], 1), (BU, 1, 1, 1)).astype(np.float32)


def group_mask():
    g_of_row = (np.arange(P) % (GD // 2)) // HALF
    return (g_of_row[:, None] == np.arange(G)[None, :]).astype(np.float32)


def cond_attention_kernel(nc, x, cond_t, w_ada_t, b_ada, w_q_t, w_kd, w_kuv_t, w_o_t, tables, mask, ident, out):
    x_units = x.rearrange("(u p) d -> u p d", p=P)
    out_units = out.rearrange("(u p) d -> u p d", p=P)

    with ExitStack() as ctx:
        def sb(name, shape):
            return ctx.enter_context(nc.sbuf_tensor(name, shape, F32))

        def bank(name):
            return ctx.enter_context(nc.psum_tensor(name, [P, 512], F32))

        def sem(name):
            return ctx.enter_context(nc.semaphore(name))

        ident_sb = sb("ident_sb", [P, P])
        tab_sb = sb("tab_sb", [P, 2, 2, GD])
        mask_sb = sb("mask_sb", [P, G])
        cond_sb = sb("cond_sb", [P, KT, B])
        w_ada_sb = sb("w_ada_sb", [P, KT, 2 * D])
        b_ada_sb = sb("b_ada_sb", [P, 2 * KT])
        w_kd_sb = sb("w_kd_sb", [LATENT, D])
        w_kuv_sb = sb("w_kuv_sb", [LATENT, 2 * GD])
        w_qkv_sb = sb("w_qkv_sb", [P, KT, DQ + 2 * GD])
        w_o_sb = sb("w_o_sb", [P, 2, D])
        scale1_sb = sb("scale1_sb", [P, KT, B])
        shift_sb = sb("shift_sb", [P, KT, B])
        x_sb = sb("x_sb", [P, UNITS, D])
        bn_sb = sb("bn_sb", [P, 2, 6])
        mv_sb = sb("mv_sb", [P, 2, 2])
        veps_sb = sb("veps_sb", [P, 2, 1])
        const_sb = sb("const_sb", [P, 2])
        rstd_sb = sb("rstd_sb", [P, 2, 1])
        xhat_sb = sb("xhat_sb", [P, 2, D])
        h_sb = sb("h_sb", [P, 2, KT, P])
        q_rope_sb = sb("q_rope_sb", [P, 2, J, 2, GD])
        k_rope_sb = sb("k_rope_sb", [P, 2, 2, GD])
        k_swap_sb = sb("k_swap_sb", [P, 2, 2, GD])
        v_sb = sb("v_sb", [P, 2, GD])
        q_t_sb = sb("q_t_sb", [P, 2, BU, J, T])
        k_bd_sb = sb("k_bd_sb", [P, 2, BU, G, T])
        v_bd_sb = sb("v_bd_sb", [P, 2, BU, G, HD])
        prob_sb = sb("prob_sb", [P, 2, BU * G, T])
        max_sb = sb("max_sb", [P, 2, BU * G])
        sum_sb = sb("sum_sb", [P, 2, BU * G])
        inv_sb = sb("inv_sb", [P, 2, BU * G])
        prob_t_sb = sb("prob_t_sb", [P, 2, BU, P])
        y_sb = sb("y_sb", [P, 2, 2, BU, T])

        xt_ps = bank("xt_ps")
        qkv_ps = bank("qkv_ps")
        qt_ps = bank("qt_ps")
        kt_ps = bank("kt_ps")
        s_ps = bank("s_ps")
        pt_ps = bank("pt_ps")
        yt_ps = bank("yt_ps")
        o_ps = bank("o_ps")

        ident_in, ada_in, kv_in, tab_in, w_in = (sem(n) for n in ("ident_in", "ada_in", "kv_in", "tab_in", "w_in"))
        zeroed = sem("zeroed")
        ada_done = sem("ada_done")
        mod_ready = sem("mod_ready")
        kv_done = sem("kv_done")
        w_ready = sem("w_ready")
        x_in = [sem("x_in_even"), sem("x_in_odd")]
        bn_done = sem("bn_done")
        stats_done = sem("stats_done")
        veps_done = sem("veps_done")
        rstd_done = sem("rstd_done")
        norm_done = sem("norm_done")
        xt_done = sem("xt_done")
        mod_done = sem("mod_done")
        h_done = sem("h_done")
        qkv_done = sem("qkv_done")
        rope_done = sem("rope_done")
        k_rope_done = sem("k_rope_done")
        v_read = sem("v_read")
        qt_done = sem("qt_done")
        qt_read = sem("qt_read")
        k_bd_done = sem("k_bd_done")
        v_bd_done = sem("v_bd_done")
        s_done = sem("s_done")
        max_done = sem("max_done")
        sub_done = sem("sub_done")
        exp_done = sem("exp_done")
        sum_done = sem("sum_done")
        inv_done = sem("inv_done")
        prob_done = sem("prob_done")
        pt_done = sem("pt_done")
        pt_read = sem("pt_read")
        yt_done = sem("yt_done")
        yt_read = sem("yt_read")
        o_done = sem("o_done")
        res_done = sem("res_done")
        stored = sem("stored")

        def has(u):
            return not isinstance(u, int) or 0 <= u < UNITS

        def later(u, n):
            return not isinstance(u, int) or u >= n

        def steps(eng, step):
            for i in range(FIRST, FIRST_FULL):
                step(i, i % 2)
            with eng.Fori(FIRST_FULL // 2, LAST_FULL // 2) as pair:
                step(pair * 2, 0)
                step(pair * 2 + 1, 1)
            for i in range(LAST_FULL, LAST):
                step(i, i % 2)

        block = ctx.enter_context(nc.Block())

        @block.sync
        def _(sp):
            def load(u, p):
                if later(u, 2):
                    sp.wait_ge(x_in[p], 8 * (u - p))
                sp.dma_start(x_sb[:, bass.ds(u, 1), :], x_units[bass.ds(u, 1)].rearrange("u p d -> p u d")).then_inc(x_in[p], 16)

            def store(u):
                sp.wait_ge(res_done, u + 1)
                sp.dma_start(out_units[bass.ds(u, 1)].rearrange("u p d -> p u d"), x_sb[:, bass.ds(u, 1), :]).then_inc(stored, 16)

            load(0, 0)
            sp.dma_start(ident_sb[:], ident).then_inc(ident_in, 16)
            load(1, 1)
            sp.dma_start(w_qkv_sb[:, :, 0:DQ], w_q_t).then_inc(w_in, 16)
            for u in range(2, LOAD_AHEAD):
                load(u, u % 2)
            sp.dma_start(w_o_sb[:], w_o_t).then_inc(w_in, 16)
            with sp.Fori(0, (UNITS - LOAD_AHEAD) // 2) as pair:
                for p in range(2):
                    load(pair * 2 + (LOAD_AHEAD + p), p)
                    store(pair * 2 + p)
            with sp.Fori(UNITS - LOAD_AHEAD, UNITS) as u:
                store(u)
            sp.wait_ge(stored, 16 * UNITS)

        @block.gpsimd
        def _(pool):
            pool.memset(v_bd_sb[:], 0.0).then_inc(zeroed, 1)
            pool.memset(const_sb[:, 0:1], EPS).then_inc(zeroed, 1)
            pool.memset(const_sb[:, 1:2], -0.5).then_inc(zeroed, 1)
            pool.wait_ge(zeroed, 3)

            def rstd(u, p):
                pool.wait_ge(stats_done, u + 1)
                if later(u, 2):
                    pool.wait_ge(norm_done, u - 1)
                pool.tensor_tensor(veps_sb[:, p], mv_sb[:, p, 1:2], const_sb[:, 0:1], ALU.add).then_inc(veps_done, 1)
                pool.wait_ge(veps_done, u + 1)
                pool.tensor_tensor(rstd_sb[:, p], veps_sb[:, p], const_sb[:, 1:2], ALU.pow).then_inc(rstd_done, 1)

            def shift(u, p):
                pool.wait_ge(mod_done, u + 1)
                pool.tensor_tensor(
                    h_sb[:, p].rearrange("c k (b t) -> c k b t", b=BU),
                    h_sb[:, p].rearrange("c k (b t) -> c k b t", b=BU),
                    shift_sb[:, :, bass.ds(u * BU, BU)].unsqueeze(3).broadcast_to([P, KT, BU, T]),
                    ALU.add,
                ).then_inc(h_done, 1)

            def k_sum(u, p):
                pool.wait_ge(rope_done, 3 * (u + 1))
                pool.tensor_tensor(k_rope_sb[:, p], k_rope_sb[:, p], k_swap_sb[:, p], ALU.add).then_inc(k_rope_done, 1)

            def divide(u, p):
                pool.wait_ge(inv_done, u + 1)
                pool.tensor_tensor(
                    prob_sb[:, p], prob_sb[:, p],
                    inv_sb[:, p].unsqueeze(2).broadcast_to([P, BU * G, T]), ALU.mult,
                ).then_inc(prob_done, 1)

            def step(i, p):
                if has(i + PRB):
                    divide(i + PRB, 1 - p)
                if has(i + STATS):
                    rstd(i + STATS, p)
                if has(i + QKV):
                    k_sum(i + QKV, 1 - p)
                if has(i + TR):
                    shift(i + TR, p)

            steps(pool, step)

        @block.vector
        def _(dve):
            def stats(u, p):
                dve.wait_ge(x_in[p], 8 * (u - p) + 16)
                dve.bn_stats(bn_sb[:, p], x_sb[:, bass.ds(u, 1), :].rearrange("p u d -> p (u d)")).then_inc(bn_done, 1)

            def stats_sum(u, p):
                dve.bn_aggr(mv_sb[:, p], bn_sb[:, p]).then_inc(stats_done, 1)

            def norm(u, p):
                dve.wait_ge(rstd_done, u + 1)
                if later(u, 2):
                    dve.wait_ge(xt_done, u - 1)
                dve.tensor_scalar(
                    xhat_sb[:, p], x_sb[:, bass.ds(u, 1), :].rearrange("p u d -> p (u d)"),
                    mv_sb[:, p, 0:1], rstd_sb[:, p], ALU.subtract, ALU.mult,
                ).then_inc(norm_done, 1)

            def mod(u, p):
                dve.wait_ge(xt_done, u + 1)
                if later(u, 2):
                    dve.wait_ge(qkv_done, u - 1)
                dve.tensor_tensor(
                    h_sb[:, p].rearrange("c k (b t) -> c k b t", b=BU),
                    xt_ps[:, 0:D].rearrange("c (k b t) -> c k b t", k=KT, b=BU),
                    scale1_sb[:, :, bass.ds(u * BU, BU)].unsqueeze(3).broadcast_to([P, KT, BU, T]),
                    ALU.mult,
                ).then_inc(mod_done, 1)

            def rope(u, p):
                dve.wait_ge(qkv_done, u + 1)
                if later(u, 2):
                    dve.wait_ge(qt_done, u - 1)
                q = qkv_ps[:, 0:DQ].rearrange("p (j c) -> p j c", j=J)
                k = qkv_ps[:, DQ:DQ + GD]
                dve.tensor_tensor(
                    k_rope_sb[:, p], k.unsqueeze(1).broadcast_to([P, 2, GD]), tab_sb[:, 0], ALU.mult,
                ).then_inc(rope_done, 1)
                for half in range(2):
                    here, other = (slice(h * GD // 2, (h + 1) * GD // 2) for h in (half, 1 - half))
                    last = dve.tensor_tensor(
                        k_swap_sb[:, p, :, here], k[:, other].unsqueeze(1).broadcast_to([P, 2, GD // 2]),
                        tab_sb[:, 1, :, here], ALU.mult,
                    )
                last.then_inc(rope_done, 1)
                dve.tensor_tensor(
                    q_rope_sb[:, p].rearrange("p j s c -> p s j c"),
                    q.unsqueeze(1).broadcast_to([P, 2, J, GD]),
                    tab_sb[:, 0].unsqueeze(2).broadcast_to([P, 2, J, GD]), ALU.mult,
                ).then_inc(rope_done, 1)

            def softmax_in(u, p):
                dve.wait_ge(s_done, u + 1)
                scores = s_ps[:, :].rearrange("p (r s) -> p r s", s=T)
                dve.tensor_reduce(max_sb[:, p], scores, AX.X, ALU.max).then_inc(max_done, 1)
                dve.wait_ge(max_done, u + 1)
                if later(u, 2):
                    dve.wait_ge(pt_done, u - 1)
                dve.tensor_tensor(
                    prob_sb[:, p], scores, max_sb[:, p].unsqueeze(2).broadcast_to([P, BU * G, T]), ALU.subtract,
                ).then_inc(sub_done, 1)

            def softmax_sum(u, p):
                dve.wait_ge(exp_done, u + 1)
                dve.tensor_reduce(sum_sb[:, p], prob_sb[:, p], AX.X, ALU.add).then_inc(sum_done, 1)
                dve.wait_ge(sum_done, u + 1)
                dve.reciprocal(inv_sb[:, p], sum_sb[:, p]).then_inc(inv_done, 1)

            def residual(u):
                dve.wait_ge(o_done, u + 1)
                row = x_sb[:, bass.ds(u, 1), :].rearrange("p u d -> p (u d)")
                dve.tensor_tensor(row, o_ps[:, 0:D], row, ALU.add).then_inc(res_done, 1)

            def modulation():
                dve.wait_ge(ada_done, 1)
                dve.wait_ge(ada_in, 48)
                for k in range(KT):
                    dve.tensor_scalar(scale1_sb[:, k], s_ps[:, k * P:(k + 1) * P], b_ada_sb[:, k:k + 1], 1.0,
                                      ALU.add, ALU.add).then_inc(mod_ready, 1)
                    dve.tensor_scalar(shift_sb[:, k], s_ps[:, (KT + k) * P:(KT + k + 1) * P],
                                      b_ada_sb[:, KT + k:KT + k + 1], None, ALU.add).then_inc(mod_ready, 1)
                dve.wait_ge(mod_ready, 2 * KT)
                dve.wait_ge(tab_in, 32)

            def step(i, p):
                if has(i + STATS):
                    stats(i + STATS, p)
                    dve.wait_ge(bn_done, i + STATS + 1)
                if has(i + NORM):
                    norm(i + NORM, 1 - p)
                if has(i + STATS):
                    stats_sum(i + STATS, p)
                if has(i + QKV):
                    rope(i + QKV, 1 - p)
                if has(i + ATT):
                    softmax_in(i + ATT, p)
                if isinstance(i, int) and i + TR == 0:
                    modulation()
                if has(i + TR):
                    mod(i + TR, p)
                if has(i + OUT):
                    residual(i + OUT)
                if has(i + ATT):
                    softmax_sum(i + ATT, p)

            steps(dve, step)

        @block.scalar
        def _(act):
            act.dma_start(cond_sb[:], cond_t).then_inc(ada_in, 16)
            act.dma_start(w_ada_sb[:], w_ada_t).then_inc(ada_in, 16)
            act.dma_start(b_ada_sb[:], b_ada).then_inc(ada_in, 16)
            act.dma_start(w_kd_sb[:], w_kd).then_inc(kv_in, 16)
            act.dma_start(w_kuv_sb[:], w_kuv_t).then_inc(kv_in, 16)
            act.dma_start(tab_sb[:], tables).then_inc(tab_in, 16)
            act.dma_start(mask_sb[:], mask).then_inc(tab_in, 16)
            act.wait_ge(kv_done, 1)
            act.activation(w_qkv_sb[:, :, DQ:], pt_ps[:, 0:KT * 2 * GD].rearrange("p (k n) -> p k n", k=KT),
                           ACT.Copy).then_inc(w_ready, 1)
            act.wait_ge(tab_in, 32)
            act.wait_ge(zeroed, 1)

            def y_out(u, p):
                act.wait_ge(yt_done, u + 1)
                if later(u, 2):
                    act.wait_ge(o_done, u - 1)
                heads = yt_ps[0:GD, :].rearrange("c (b j l t) -> c j l b t", b=BU, j=2, l=2)
                for half in range(2):
                    last = act.activation(y_sb[half * GD:(half + 1) * GD, p], heads[:, half], ACT.Copy)
                last.then_inc(yt_read, 1)

            def v_out(u, p):
                act.wait_ge(rope_done, 3 * (u + 1))
                if later(u, 2):
                    act.wait_ge(v_bd_done, u - 1)
                act.activation(v_sb[:, p], qkv_ps[:, DQ + GD:DQ + 2 * GD], ACT.Copy).then_inc(v_read, 1)

            def v_spread(u, p):
                act.wait_ge(v_read, u + 1)
                if later(u, 2):
                    act.wait_ge(yt_done, u - 1)
                for b in range(BU):
                    for g in range(G):
                        last = act.activation(
                            v_bd_sb[g * T:(g + 1) * T, p, b, g], v_sb[b * T:(b + 1) * T, p, g * HD:(g + 1) * HD], ACT.Copy)
                last.then_inc(v_bd_done, 1)

            def pt_out(u, p):
                act.wait_ge(pt_done, u + 1)
                if later(u, 2):
                    act.wait_ge(yt_done, u - 1)
                act.activation(prob_t_sb[:, p], pt_ps[:, :].rearrange("p (b q) -> p b q", b=BU), ACT.Copy).then_inc(pt_read, 1)

            def exps(u, p):
                act.wait_ge(sub_done, u + 1)
                act.activation(prob_sb[:, p], prob_sb[:, p], ACT.Exp, scale=SCALE).then_inc(exp_done, 1)

            def qk_out(u, p):
                act.wait_ge(qt_done, u + 1)
                if later(u, 2):
                    act.wait_ge(s_done, u - 1)
                act.activation(q_t_sb[:, p].rearrange("c b j t -> c j b t"),
                               qt_ps[:, :].rearrange("c (j b t) -> c j b t", j=J, b=BU), ACT.Copy).then_inc(qt_read, 1)
                for g in range(G):
                    last = act.activation(k_bd_sb[:, p, :, g], kt_ps[:, 0:P].rearrange("c (b t) -> c b t", b=BU),
                                          ACT.Copy, scale=mask_sb[:, g:g + 1])
                last.then_inc(k_bd_done, 1)

            def step(i, p):
                if has(i + OUT):
                    y_out(i + OUT, p)
                if has(i + ATT):
                    v_spread(i + ATT, p)
                if has(i + QKV):
                    v_out(i + QKV, 1 - p)
                if has(i + PRB):
                    pt_out(i + PRB, 1 - p)
                if has(i + ATT):
                    exps(i + ATT, p)
                if has(i + QKV):
                    qk_out(i + QKV, 1 - p)

            steps(act, step)

        @block.tensor
        def _(pe):
            pe.wait_ge(ada_in, 48)
            for m in range(2 * KT):
                for k in range(KT):
                    last = pe.matmul(s_ps[:, m * P:(m + 1) * P], w_ada_sb[:, k, m * P:(m + 1) * P], cond_sb[:, k],
                                     start=(k == 0), stop=(k == KT - 1))
            last.then_inc(ada_done, 1)
            pe.wait_ge(kv_in, 32)
            for k in range(KT):
                last = pe.matmul(pt_ps[:, k * 2 * GD:(k + 1) * 2 * GD], w_kd_sb[:, k * P:(k + 1) * P], w_kuv_sb[:],
                                 start=True, stop=True)
            last.then_inc(kv_done, 1)
            pe.wait_ge(ident_in, 16)

            def qkv(u, p):
                if isinstance(u, int) and u == 0:
                    pe.wait_ge(w_in, 32)
                    pe.wait_ge(w_ready, 1)
                pe.wait_ge(h_done, u + 1)
                if later(u, 1):
                    pe.wait_ge(v_read, u)
                for k in range(KT):
                    last = pe.matmul(qkv_ps[:, 0:DQ + 2 * GD], h_sb[:, p, k], w_qkv_sb[:, k], start=(k == 0), stop=(k == KT - 1))
                last.then_inc(qkv_done, 1)

            def scores(u, p):
                pe.wait_ge(qt_read, u + 1)
                pe.wait_ge(k_bd_done, u + 1)
                if later(u, 1):
                    pe.wait_ge(sub_done, u)
                else:
                    pe.wait_ge(mod_ready, 2 * KT)
                for b in range(BU):
                    last = pe.matmul(s_ps[:, b * P:(b + 1) * P], q_t_sb[:, p, b].rearrange("c j t -> c (j t)"),
                                     k_bd_sb[:, p, b].rearrange("c g t -> c (g t)"), start=True, stop=True)
                last.then_inc(s_done, 1)

            def prob_t(u, p):
                pe.wait_ge(prob_done, u + 1)
                if later(u, 1):
                    pe.wait_ge(pt_read, u)
                else:
                    pe.wait_ge(w_ready, 1)
                for b in range(BU):
                    last = pe.transpose(pt_ps[:, b * P:(b + 1) * P],
                                        prob_sb[:, p, b * G:(b + 1) * G].rearrange("p g t -> p (g t)"), ident_sb[:])
                last.then_inc(pt_done, 1)

            def xhat_t(u, p):
                pe.wait_ge(norm_done, u + 1)
                if later(u, 1):
                    pe.wait_ge(mod_done, u)
                for k in range(KT):
                    last = pe.transpose(xt_ps[:, k * P:(k + 1) * P], xhat_sb[:, p, k * P:(k + 1) * P], ident_sb[:])
                last.then_inc(xt_done, 1)

            def project(u, p):
                pe.wait_ge(yt_read, u + 1)
                if later(u, 1):
                    pe.wait_ge(res_done, u)
                for l in range(2):
                    last = pe.matmul(o_ps[:, 0:D], y_sb[:, p, l].rearrange("c b t -> c (b t)"), w_o_sb[:, l],
                                     start=(l == 0), stop=(l == 1))
                last.then_inc(o_done, 1)

            def qk_t(u, p):
                pe.wait_ge(rope_done, 3 * (u + 1))
                if later(u, 1):
                    pe.wait_ge(qt_read, u)
                    pe.wait_ge(k_bd_done, u)
                for j in range(J):
                    pe.transpose(qt_ps[:, j * P:(j + 1) * P], q_rope_sb[:, p, j].rearrange("p s c -> p (s c)"), ident_sb[:])
                pe.wait_ge(k_rope_done, u + 1)
                pe.transpose(kt_ps[:, 0:P], k_rope_sb[:, p].rearrange("p s c -> p (s c)"), ident_sb[:]).then_inc(qt_done, 1)

            def heads_out(u, p):
                pe.wait_ge(pt_read, u + 1)
                pe.wait_ge(v_bd_done, u + 1)
                if later(u, 1):
                    pe.wait_ge(yt_read, u)
                for b in range(BU):
                    last = pe.matmul(yt_ps[0:GD, b * P:(b + 1) * P], v_bd_sb[:, p, b].rearrange("c g d -> c (g d)"),
                                     prob_t_sb[:, p, b], start=True, stop=True)
                last.then_inc(yt_done, 1)

            def step(i, p):
                if has(i + QKV):
                    qkv(i + QKV, 1 - p)
                if has(i + ATT):
                    scores(i + ATT, p)
                if has(i + PRB):
                    prob_t(i + PRB, 1 - p)
                if has(i + TR):
                    xhat_t(i + TR, p)
                if has(i + OUT):
                    project(i + OUT, p)
                if has(i + QKV):
                    qk_t(i + QKV, 1 - p)
                if has(i + PRB):
                    heads_out(i + PRB, 1 - p)

            steps(pe, step)


def kernel(x, cond_2048, L0_cond_W_ada, L0_cond_b_ada, L0_cond_Wq, L0_cond_Wkd, L0_cond_Wku, L0_cond_Wvu, L0_cond_Wo):
    import concourse.bacc as bacc
    from concourse.bass_utils import run_bass_kernel_spmd

    contig = np.ascontiguousarray
    by_tile = lambda w: contig(w.reshape(KT, P, -1).transpose(1, 0, 2))
    w_q, w_ku, w_vu, w_o = (np.asarray(w) for w in (L0_cond_Wq, L0_cond_Wku, L0_cond_Wvu, L0_cond_Wo))
    w_q_t = w_q.reshape(G, J, 2, HALF, D).transpose(4, 1, 2, 0, 3).reshape(D, DQ)
    w_ku_t = w_ku.reshape(G, 2, HALF, LATENT).transpose(3, 1, 0, 2).reshape(LATENT, GD)
    w_o_t = w_o.reshape(D, G, 2, 2, HD).transpose(2, 1, 4, 3, 0).reshape(P, 2, D)
    arrays = {
        "x": np.asarray(x).reshape(B * T, D),
        "cond_t": by_tile(np.asarray(cond_2048).T),
        "w_ada_t": by_tile(np.asarray(L0_cond_W_ada).T),
        "b_ada": contig(np.asarray(L0_cond_b_ada).reshape(2 * KT, P).T),
        "w_q_t": by_tile(w_q_t),
        "w_kd": np.asarray(L0_cond_Wkd),
        "w_kuv_t": contig(np.concatenate([w_ku_t, w_vu.T], axis=1)),
        "w_o_t": contig(w_o_t),
        "tables": rope_tables(),
        "mask": group_mask(),
        "ident": np.eye(P, dtype=np.float32),
    }
    nc = bacc.Bacc("TRN2", target_bir_lowering=False, num_devices=1)
    args = [nc.dram_tensor(n, a.shape, F32, kind="ExternalInput").ap() for n, a in arrays.items()]
    out = nc.dram_tensor("out", (B * T, D), F32, kind="ExternalOutput").ap()
    cond_attention_kernel(nc, *args, out)
    r = run_bass_kernel_spmd(nc, [arrays], core_ids=[0])
    return r.results[0]["out"].reshape(B, T, D)
```

```python
from contextlib import ExitStack

import numpy as np

import concourse.bass as bass
from concourse import mybir

F32 = mybir.dt.float32
F32R = mybir.dt.float32r
ALU = mybir.AluOpType
ACT = mybir.ActivationFunctionType
AX = mybir.AxisListType

P = 128
B, T, D = 128, 32, 256
HQ, G, HD = 16, 4, 16
J = HQ // G
HALF = HD // 2
LATENT = 64
EPS = 1e-5
THETA = 10000.0
SCALE = float(HD) ** -0.5
BU = P // T
UNITS = B * T // P
KT = D // P
GD = G * HD
DQ = HQ * HD
LOAD_AHEAD = 8

STATS, NORM, TR, MOD, QKV, ATT, PRB, OUT, RES = 4, 3, 3, 2, 1, 0, -1, -2, -3
BODY = 4
FIRST_FULL = 4
LAST_FULL = UNITS - STATS
FIRST, LAST = -STATS, UNITS - RES


def rope_tables():
    freqs = (1.0 / np.float32(THETA) ** (np.arange(0, HD, 2, dtype=np.float32) / np.float32(HD))).astype(np.float32)
    emb = np.arange(T, dtype=np.float32)[:, None] * freqs[None, :]
    cos, sin = np.cos(emb).astype(np.float32), np.sin(emb).astype(np.float32)
    halves = lambda first, second: np.concatenate([first, second], 1)
    plain = np.stack([halves(cos, cos), halves(sin, sin)], 1)
    swap = np.stack([halves(-sin, sin), halves(cos, -cos)], 1)
    return np.tile(np.stack([plain, swap], 1), (BU, 1, 1, 1)).astype(np.float32)


def cond_attention_kernel(nc, x, cond_t, w_ada_t, b_ada, w_q_t, w_kd, w_kuv_t, w_o_t, tables, ident, out):
    x_units = x.rearrange("(u p) d -> u p d", p=P)
    out_units = out.rearrange("(u p) d -> u p d", p=P)

    with ExitStack() as ctx:
        def sb(name, shape, dtype=F32):
            return ctx.enter_context(nc.sbuf_tensor(name, shape, dtype))

        def bank(name):
            return ctx.enter_context(nc.psum_tensor(name, [P, 512], F32))

        def sem(name):
            return ctx.enter_context(nc.semaphore(name))

        ident_sb = sb("ident_sb", [P, P])
        tab_sb = sb("tab_sb", [P, 2, 2, HD])
        cond_sb = sb("cond_sb", [P, KT, B])
        w_ada_sb = sb("w_ada_sb", [P, KT, 2 * D])
        b_ada_sb = sb("b_ada_sb", [P, 2 * KT])
        w_kd_sb = sb("w_kd_sb", [LATENT, D])
        w_kuv_sb = sb("w_kuv_sb", [LATENT, 2 * GD])
        w_qkv_sb = sb("w_qkv_sb", [P, KT, DQ + 2 * GD])
        w_hi_sb = sb("w_hi_sb", [P, KT, DQ + 2 * GD], F32R)
        w_lo_sb = sb("w_lo_sb", [P, KT, DQ + 2 * GD], F32R)
        w_o_sb = sb("w_o_sb", [P, 2, D])
        scale1_sb = sb("scale1_sb", [P, KT, B])
        shift_sb = sb("shift_sb", [P, KT, B])
        x_sb = sb("x_sb", [P, UNITS, D])
        bn_sb = sb("bn_sb", [P, 2, 6])
        mv_sb = sb("mv_sb", [P, 2, 2])
        veps_sb = sb("veps_sb", [P, 2, 1])
        const_sb = sb("const_sb", [P, 2])
        rstd_sb = sb("rstd_sb", [P, 2, 1])
        xhat_sb = sb("xhat_sb", [P, 2, D])
        h_sb = sb("h_sb", [P, 2, KT, P])
        h_hi_sb = sb("h_hi_sb", [P, 2, KT, P], F32R)
        h_lo_sb = sb("h_lo_sb", [P, 2, KT, P], F32R)
        q_rope_sb = sb("q_rope_sb", [P, 2, J * G, 2, HD])
        k_sb = sb("k_sb", [P, 2, GD])
        k_rope_sb = sb("k_rope_sb", [P, 2, G, 2, HD])
        k_swap_sb = sb("k_swap_sb", [P, 2, G, 2, HD])
        q_t_sb = sb("q_t_sb", [P, 2, BU, J, T])
        k_bd_sb = sb("k_bd_sb", [P, 2, BU, G, T])
        v_bd_sb = sb("v_bd_sb", [P, BODY, BU, G, HD])
        prob_sb = sb("prob_sb", [P, 2, BU * G, T])
        max_sb = sb("max_sb", [P, 2, BU * G])
        sum_sb = sb("sum_sb", [P, 2, BU * G])
        inv_sb = sb("inv_sb", [P, 2, BU * G])
        prob_t_sb = sb("prob_t_sb", [P, 2, BU, P])
        y_sb = sb("y_sb", [P, 2, 2, BU, T])

        xt_ps = bank("xt_ps")
        qkv_ps = bank("qkv_ps")
        qt_ps = bank("qt_ps")
        kt_ps = bank("kt_ps")
        s_ps = bank("s_ps")
        pt_ps = bank("pt_ps")
        yt_ps = bank("yt_ps")
        o_ps = bank("o_ps")

        ident_in, ada_in, kv_in, tab_in, w_in = (sem(n) for n in ("ident_in", "ada_in", "kv_in", "tab_in", "w_in"))
        const_ready = sem("const_ready")
        zeroed = sem("zeroed")
        ada_done = sem("ada_done")
        mod_ready = sem("mod_ready")
        kv_done = sem("kv_done")
        w_ready = sem("w_ready")
        w_hi_done = sem("w_hi_done")
        w_lo_done = sem("w_lo_done")
        x_in = [sem("x_in_even"), sem("x_in_odd")]
        bn_done = sem("bn_done")
        stats_done = sem("stats_done")
        veps_done = sem("veps_done")
        rstd_done = sem("rstd_done")
        norm_done = sem("norm_done")
        xt_done = sem("xt_done")
        mod_done = sem("mod_done")
        h_done = sem("h_done")
        h_hi_done = sem("h_hi_done")
        h_lo_done = sem("h_lo_done")
        qkv_done = sem("qkv_done")
        rope_done = sem("rope_done")
        k_read = sem("k_read")
        k_parts_done = sem("k_parts_done")
        k_rope_done = sem("k_rope_done")
        qt_done = sem("qt_done")
        qt_read = sem("qt_read")
        k_bd_done = sem("k_bd_done")
        v_bd_done = sem("v_bd_done")
        s_done = sem("s_done")
        max_done = sem("max_done")
        sub_done = sem("sub_done")
        exp_done = sem("exp_done")
        sum_done = sem("sum_done")
        inv_done = sem("inv_done")
        prob_done = sem("prob_done")
        pt_done = sem("pt_done")
        pt_read = sem("pt_read")
        yt_done = sem("yt_done")
        yt_read = sem("yt_read")
        o_done = sem("o_done")
        res_done = sem("res_done")
        stored = sem("stored")

        def has(u):
            return not isinstance(u, int) or 0 <= u < UNITS

        def later(u, n):
            return not isinstance(u, int) or u >= n

        def steps(eng, step):
            for i in range(FIRST, FIRST_FULL):
                step(i, i % BODY)
            with eng.Fori(FIRST_FULL // BODY, LAST_FULL // BODY) as four:
                for s in range(BODY):
                    step(four * BODY + s, s)
            for i in range(LAST_FULL, LAST):
                step(i, i % BODY)

        block = ctx.enter_context(nc.Block())

        @block.sync
        def _(sp):
            def load(u, p):
                if later(u, 2):
                    sp.wait_ge(x_in[p], 8 * (u - p))
                sp.dma_start(x_sb[:, bass.ds(u, 1), :], x_units[bass.ds(u, 1)].rearrange("u p d -> p u d")).then_inc(x_in[p], 16)

            def store(u):
                sp.wait_ge(res_done, u + 1)
                sp.dma_start(out_units[bass.ds(u, 1)].rearrange("u p d -> p u d"), x_sb[:, bass.ds(u, 1), :]).then_inc(stored, 16)

            load(0, 0)
            sp.dma_start(w_kd_sb[:], w_kd).then_inc(kv_in, 16)
            sp.dma_start(w_kuv_sb[:], w_kuv_t).then_inc(kv_in, 16)
            sp.dma_start(ident_sb[:], ident).then_inc(ident_in, 16)
            load(1, 1)
            sp.dma_start(w_qkv_sb[:, :, 0:DQ], w_q_t).then_inc(w_in, 16)
            for u in range(2, LOAD_AHEAD):
                load(u, u % 2)
            sp.dma_start(w_o_sb[:], w_o_t).then_inc(w_in, 16)
            with sp.Fori(0, (UNITS - LOAD_AHEAD) // 2) as pair:
                for p in range(2):
                    load(pair * 2 + (LOAD_AHEAD + p), p)
                    store(pair * 2 + p)
            with sp.Fori(UNITS - LOAD_AHEAD, UNITS) as u:
                store(u)
            sp.wait_ge(stored, 16 * UNITS)

        @block.gpsimd
        def _(pool):
            pool.memset(const_sb[:, 0:1], EPS).then_inc(const_ready, 1)
            pool.memset(const_sb[:, 1:2], -0.5).then_inc(const_ready, 1)
            pool.memset(v_bd_sb[:], 0.0).then_inc(zeroed, 1)
            pool.memset(k_bd_sb[:], 0.0).then_inc(zeroed, 1)
            pool.wait_ge(const_ready, 2)

            def rstd(u, p):
                pool.wait_ge(stats_done, u + 1)
                if later(u, 2):
                    pool.wait_ge(norm_done, u - 1)
                pool.tensor_tensor(veps_sb[:, p], mv_sb[:, p, 1:2], const_sb[:, 0:1], ALU.add).then_inc(veps_done, 1)
                pool.wait_ge(veps_done, u + 1)
                pool.tensor_tensor(rstd_sb[:, p], veps_sb[:, p], const_sb[:, 1:2], ALU.pow).then_inc(rstd_done, 1)

            def shift(u, p):
                pool.wait_ge(mod_done, u + 1)
                pool.tensor_tensor(
                    h_sb[:, p].rearrange("c k (b t) -> c k b t", b=BU),
                    h_sb[:, p].rearrange("c k (b t) -> c k b t", b=BU),
                    shift_sb[:, :, bass.ds(u * BU, BU)].unsqueeze(3).broadcast_to([P, KT, BU, T]),
                    ALU.add,
                ).then_inc(h_done, 1)

            def k_rope(u, p):
                if isinstance(u, int) and u == 0:
                    pool.wait_ge(tab_in, 16)
                pool.wait_ge(k_read, u + 1)
                if later(u, 2):
                    pool.wait_ge(qt_done, u - 1)
                k = k_sb[:, p].rearrange("p (g h i) -> p g h i", g=G, h=2)
                pool.tensor_tensor(
                    k_rope_sb[:, p].rearrange("p g s c -> p s g c"),
                    k_sb[:, p].rearrange("p (g c) -> p g c", g=G).unsqueeze(1).broadcast_to([P, 2, G, HD]),
                    tab_sb[:, 0].unsqueeze(2).broadcast_to([P, 2, G, HD]), ALU.mult,
                ).then_inc(k_parts_done, 1)
                for half in range(2):
                    here = slice(half * HALF, (half + 1) * HALF)
                    pool.tensor_tensor(
                        k_swap_sb[:, p, :, :, here].rearrange("p g s i -> p s g i"),
                        k[:, :, 1 - half].unsqueeze(1).broadcast_to([P, 2, G, HALF]),
                        tab_sb[:, 1, :, here].unsqueeze(2).broadcast_to([P, 2, G, HALF]), ALU.mult,
                    ).then_inc(k_parts_done, 1)
                pool.wait_ge(k_parts_done, 3 * (u + 1))
                pool.tensor_tensor(k_rope_sb[:, p], k_rope_sb[:, p], k_swap_sb[:, p], ALU.add).then_inc(k_rope_done, 1)

            def divide(u, p):
                pool.wait_ge(inv_done, u + 1)
                pool.tensor_tensor(
                    prob_sb[:, p], prob_sb[:, p],
                    inv_sb[:, p].unsqueeze(2).broadcast_to([P, BU * G, T]), ALU.mult,
                ).then_inc(prob_done, 1)

            def step(i, s):
                p = s % 2
                if has(i + MOD):
                    shift(i + MOD, p)
                if has(i + STATS):
                    rstd(i + STATS, p)
                if has(i + PRB):
                    divide(i + PRB, 1 - p)
                if has(i + QKV):
                    k_rope(i + QKV, 1 - p)

            steps(pool, step)

        @block.vector
        def _(dve):
            def stats(u, p):
                dve.wait_ge(x_in[p], 8 * (u - p) + 16)
                dve.bn_stats(bn_sb[:, p], x_sb[:, bass.ds(u, 1), :].rearrange("p u d -> p (u d)")).then_inc(bn_done, 1)
                dve.wait_ge(bn_done, u + 1)

            def stats_sum(u, p):
                dve.bn_aggr(mv_sb[:, p], bn_sb[:, p]).then_inc(stats_done, 1)

            def norm(u, p):
                dve.wait_ge(rstd_done, u + 1)
                if later(u, 2):
                    dve.wait_ge(xt_done, u - 1)
                dve.tensor_scalar(
                    xhat_sb[:, p], x_sb[:, bass.ds(u, 1), :].rearrange("p u d -> p (u d)"),
                    mv_sb[:, p, 0:1], rstd_sb[:, p], ALU.subtract, ALU.mult,
                ).then_inc(norm_done, 1)

            def mod(u, p):
                dve.wait_ge(xt_done, u + 1)
                if later(u, 2):
                    dve.wait_ge(h_lo_done, u - 1)
                dve.tensor_tensor(
                    h_sb[:, p].rearrange("c k (b t) -> c k b t", b=BU),
                    xt_ps[:, 0:D].rearrange("c (k b t) -> c k b t", k=KT, b=BU),
                    scale1_sb[:, :, bass.ds(u * BU, BU)].unsqueeze(3).broadcast_to([P, KT, BU, T]),
                    ALU.mult,
                ).then_inc(mod_done, 1)

            def rope(u, p):
                dve.wait_ge(qkv_done, u + 1)
                if later(u, 2):
                    dve.wait_ge(qt_done, u - 1)
                dve.tensor_tensor(
                    q_rope_sb[:, p].rearrange("p r s c -> p s r c"),
                    qkv_ps[:, 0:DQ].rearrange("p (r c) -> p r c", c=HD).unsqueeze(1).broadcast_to([P, 2, J * G, HD]),
                    tab_sb[:, 0].unsqueeze(2).broadcast_to([P, 2, J * G, HD]), ALU.mult,
                ).then_inc(rope_done, 1)

            scores = s_ps[:, :].rearrange("p (r s) -> p r s", s=T)

            def row_max(u, p):
                dve.wait_ge(s_done, u + 1)
                dve.tensor_reduce(max_sb[:, p], scores, AX.X, ALU.max).then_inc(max_done, 1)

            def subtract_max(u, p):
                dve.wait_ge(max_done, u + 1)
                if later(u, 2):
                    dve.wait_ge(pt_done, u - 1)
                dve.tensor_tensor(
                    prob_sb[:, p], scores, max_sb[:, p].unsqueeze(2).broadcast_to([P, BU * G, T]), ALU.subtract,
                ).then_inc(sub_done, 1)

            def row_sum(u, p):
                dve.wait_ge(exp_done, u + 1)
                dve.tensor_reduce(sum_sb[:, p], prob_sb[:, p], AX.X, ALU.add).then_inc(sum_done, 1)

            def inverse(u, p):
                dve.wait_ge(sum_done, u + 1)
                dve.reciprocal(inv_sb[:, p], sum_sb[:, p]).then_inc(inv_done, 1)

            def h_low(u, p):
                dve.wait_ge(h_hi_done, u + 1)
                if later(u, 2):
                    dve.wait_ge(qkv_done, u - 1)
                dve.tensor_tensor(h_lo_sb[:, p], h_sb[:, p], h_hi_sb[:, p].bitcast(F32), ALU.subtract).then_inc(h_lo_done, 1)

            def residual(u):
                dve.wait_ge(o_done, u + 1)
                row = x_sb[:, bass.ds(u, 1), :].rearrange("p u d -> p (u d)")
                dve.tensor_tensor(row, o_ps[:, 0:D], row, ALU.add).then_inc(res_done, 1)

            def modulation():
                dve.wait_ge(ada_in, 48)
                dve.wait_ge(ada_done, 1)
                for k in range(KT):
                    dve.tensor_scalar(scale1_sb[:, k], s_ps[:, k * P:(k + 1) * P], b_ada_sb[:, k:k + 1], 1.0,
                                      ALU.add, ALU.add).then_inc(mod_ready, 1)
                dve.wait_ge(ada_done, 2)
                for k in range(KT):
                    dve.tensor_scalar(shift_sb[:, k], yt_ps[:, k * P:(k + 1) * P], b_ada_sb[:, KT + k:KT + k + 1], None,
                                      ALU.add).then_inc(mod_ready, 1)
                dve.wait_ge(mod_ready, 2 * KT)
                dve.wait_ge(tab_in, 16)

            def weights_low():
                dve.wait_ge(w_hi_done, 1)
                dve.tensor_tensor(w_lo_sb[:], w_qkv_sb[:], w_hi_sb[:].bitcast(F32), ALU.subtract).then_inc(w_lo_done, 1)

            def step(i, s):
                p = s % 2
                if isinstance(i, int) and i + MOD == 0:
                    weights_low()
                    modulation()
                if has(i + MOD):
                    mod(i + MOD, p)
                if has(i + STATS):
                    stats(i + STATS, p)
                if has(i + NORM):
                    norm(i + NORM, 1 - p)
                if has(i + STATS):
                    stats_sum(i + STATS, p)
                if has(i + PRB):
                    row_sum(i + PRB, 1 - p)
                if has(i + RES):
                    residual(i + RES)
                if has(i + PRB):
                    inverse(i + PRB, 1 - p)
                if has(i + QKV):
                    rope(i + QKV, 1 - p)
                if has(i + MOD):
                    h_low(i + MOD, p)
                if has(i + ATT):
                    row_max(i + ATT, p)
                if has(i + ATT):
                    subtract_max(i + ATT, p)

            steps(dve, step)

        @block.scalar
        def _(act):
            act.dma_start(w_ada_sb[:], w_ada_t).then_inc(ada_in, 16)
            act.dma_start(cond_sb[:], cond_t).then_inc(ada_in, 16)
            act.dma_start(b_ada_sb[:], b_ada).then_inc(ada_in, 16)
            act.dma_start(tab_sb[:], tables).then_inc(tab_in, 16)
            act.wait_ge(kv_done, 1)
            act.activation(w_qkv_sb[:, :, DQ:], pt_ps[:, 0:KT * 2 * GD].rearrange("p (k n) -> p k n", k=KT),
                           ACT.Copy).then_inc(w_ready, 1)
            act.wait_ge(w_in, 16)
            act.wait_ge(w_ready, 1)
            act.activation(w_hi_sb[:], w_qkv_sb[:], ACT.Copy).then_inc(w_hi_done, 1)
            act.wait_ge(zeroed, 2)

            def y_out(u, p):
                act.wait_ge(yt_done, u + 1)
                if later(u, 2):
                    act.wait_ge(o_done, u - 1)
                heads = yt_ps[0:GD, :].rearrange("c (b j l t) -> c j l b t", b=BU, j=2, l=2)
                for half in range(2):
                    last = act.activation(y_sb[half * GD:(half + 1) * GD, p], heads[:, half], ACT.Copy)
                last.then_inc(yt_read, 1)

            def k_raw_out(u, p):
                act.wait_ge(rope_done, u + 1)
                if later(u, 2):
                    act.wait_ge(k_rope_done, u - 1)
                act.activation(k_sb[:, p], qkv_ps[:, DQ:DQ + GD], ACT.Copy).then_inc(k_read, 1)

            def v_out(u, s):
                if later(u, BODY):
                    act.wait_ge(yt_done, u - (BODY - 1))
                for b in range(BU):
                    for g in range(G):
                        c = DQ + GD + g * HD
                        last = act.activation(v_bd_sb[g * T:(g + 1) * T, s, b, g], qkv_ps[b * T:(b + 1) * T, c:c + HD], ACT.Copy)
                last.then_inc(v_bd_done, 1)

            def h_high(u, p):
                act.wait_ge(h_done, u + 1)
                if later(u, 2):
                    act.wait_ge(qkv_done, u - 1)
                act.activation(h_hi_sb[:, p], h_sb[:, p], ACT.Copy).then_inc(h_hi_done, 1)

            def pt_out(u, p):
                act.wait_ge(pt_done, u + 1)
                if later(u, 2):
                    act.wait_ge(yt_done, u - 1)
                act.activation(prob_t_sb[:, p], pt_ps[:, :].rearrange("p (b q) -> p b q", b=BU), ACT.Copy).then_inc(pt_read, 1)

            def exps(u, p):
                act.wait_ge(sub_done, u + 1)
                act.activation(prob_sb[:, p], prob_sb[:, p], ACT.Exp, scale=SCALE).then_inc(exp_done, 1)

            def q_out(u, p):
                act.wait_ge(qt_done, u + 1)
                if later(u, 2):
                    act.wait_ge(s_done, u - 1)
                act.activation(q_t_sb[:, p].rearrange("c b j t -> c j b t"),
                               qt_ps[:, :].rearrange("c (j b t) -> c j b t", j=J, b=BU), ACT.Copy).then_inc(qt_read, 1)

            def k_out(u, p):
                act.wait_ge(qt_done, u + 1)
                if later(u, 2):
                    act.wait_ge(s_done, u - 1)
                for g in range(G):
                    rows = slice(g * P // G, (g + 1) * P // G)
                    last = act.activation(k_bd_sb[rows, p, :, g], kt_ps[rows, 0:P].rearrange("c (b t) -> c b t", b=BU), ACT.Copy)
                last.then_inc(k_bd_done, 1)

            def step(i, s):
                p = s % 2
                if has(i + MOD):
                    h_high(i + MOD, p)
                if has(i + QKV):
                    k_raw_out(i + QKV, 1 - p)
                if has(i + OUT):
                    y_out(i + OUT, p)
                if has(i + QKV):
                    v_out(i + QKV, (s + QKV) % BODY)
                if has(i + ATT):
                    exps(i + ATT, p)
                if has(i + PRB):
                    pt_out(i + PRB, 1 - p)
                if has(i + QKV):
                    q_out(i + QKV, 1 - p)
                if has(i + QKV):
                    k_out(i + QKV, 1 - p)

            steps(act, step)

        @block.tensor
        def _(pe):
            pe.wait_ge(kv_in, 32)
            for k in range(KT):
                last = pe.matmul(pt_ps[:, k * 2 * GD:(k + 1) * 2 * GD], w_kd_sb[:, k * P:(k + 1) * P], w_kuv_sb[:],
                                 start=True, stop=True)
            last.then_inc(kv_done, 1)
            pe.wait_ge(ada_in, 48)
            for part, ps in enumerate((s_ps, yt_ps)):
                for m in range(KT):
                    row = part * D + m * P
                    for k in range(KT):
                        last = pe.matmul(ps[:, m * P:(m + 1) * P], w_ada_sb[:, k, row:row + P], cond_sb[:, k],
                                         start=(k == 0), stop=(k == KT - 1))
                last.then_inc(ada_done, 1)
            pe.wait_ge(ident_in, 16)

            def qkv(u, p):
                if isinstance(u, int) and u == 0:
                    pe.wait_ge(w_lo_done, 1)
                pe.wait_ge(h_hi_done, u + 1)
                if later(u, 1):
                    pe.wait_ge(v_bd_done, u)
                for h, w in ((h_hi_sb, w_lo_sb), (h_lo_sb, w_hi_sb), (h_hi_sb, w_hi_sb)):
                    if h is h_lo_sb:
                        pe.wait_ge(h_lo_done, u + 1)
                    for k in range(KT):
                        last = pe.matmul(qkv_ps[:, 0:DQ + 2 * GD], h[:, p, k], w[:, k],
                                         start=(w is w_lo_sb and k == 0), stop=(w is w_hi_sb and h is h_hi_sb and k == KT - 1))
                last.then_inc(qkv_done, 1)

            def scores(u, p):
                pe.wait_ge(qt_read, u + 1)
                pe.wait_ge(k_bd_done, u + 1)
                if later(u, 1):
                    pe.wait_ge(sub_done, u)
                else:
                    pe.wait_ge(mod_ready, 2 * KT)
                for b in range(BU):
                    last = pe.matmul(s_ps[:, b * P:(b + 1) * P], q_t_sb[:, p, b].rearrange("c j t -> c (j t)"),
                                     k_bd_sb[:, p, b].rearrange("c g t -> c (g t)"), start=True, stop=True)
                last.then_inc(s_done, 1)

            def prob_t(u, p):
                pe.wait_ge(prob_done, u + 1)
                if later(u, 1):
                    pe.wait_ge(pt_read, u)
                else:
                    pe.wait_ge(w_ready, 1)
                for b in range(BU):
                    last = pe.transpose(pt_ps[:, b * P:(b + 1) * P],
                                        prob_sb[:, p, b * G:(b + 1) * G].rearrange("p g t -> p (g t)"), ident_sb[:])
                last.then_inc(pt_done, 1)

            def xhat_t(u, p):
                pe.wait_ge(norm_done, u + 1)
                if later(u, 1):
                    pe.wait_ge(mod_done, u)
                for k in range(KT):
                    last = pe.transpose(xt_ps[:, k * P:(k + 1) * P], xhat_sb[:, p, k * P:(k + 1) * P], ident_sb[:])
                last.then_inc(xt_done, 1)

            def project(u, p):
                pe.wait_ge(yt_read, u + 1)
                if later(u, 1):
                    pe.wait_ge(res_done, u)
                else:
                    pe.wait_ge(w_in, 32)
                for l in range(2):
                    last = pe.matmul(o_ps[:, 0:D], y_sb[:, p, l].rearrange("c b t -> c (b t)"), w_o_sb[:, l],
                                     start=(l == 0), stop=(l == 1))
                last.then_inc(o_done, 1)

            def qk_t(u, p):
                pe.wait_ge(rope_done, u + 1)
                if later(u, 1):
                    pe.wait_ge(qt_read, u)
                    pe.wait_ge(k_bd_done, u)
                for j in range(J):
                    pe.transpose(qt_ps[:, j * P:(j + 1) * P], q_rope_sb[:, p, j * G:(j + 1) * G].rearrange("p g s c -> p (g s c)"), ident_sb[:])
                pe.wait_ge(k_rope_done, u + 1)
                pe.transpose(kt_ps[:, 0:P], k_rope_sb[:, p].rearrange("p g s c -> p (g s c)"), ident_sb[:]).then_inc(qt_done, 1)

            def heads_out(u, p, s):
                pe.wait_ge(pt_read, u + 1)
                pe.wait_ge(v_bd_done, u + 1)
                if later(u, 1):
                    pe.wait_ge(yt_read, u)
                for b in range(BU):
                    last = pe.matmul(yt_ps[0:GD, b * P:(b + 1) * P], v_bd_sb[:, s, b].rearrange("c g d -> c (g d)"),
                                     prob_t_sb[:, p, b], start=True, stop=True)
                last.then_inc(yt_done, 1)

            def step(i, s):
                p = s % 2
                if has(i + QKV):
                    qkv(i + QKV, 1 - p)
                if has(i + OUT):
                    heads_out(i + OUT, p, (s + OUT) % BODY)
                if has(i + ATT):
                    scores(i + ATT, p)
                if has(i + TR):
                    xhat_t(i + TR, 1 - p)
                if has(i + OUT):
                    project(i + OUT, p)
                if has(i + PRB):
                    prob_t(i + PRB, 1 - p)
                if has(i + QKV):
                    qk_t(i + QKV, 1 - p)

            steps(pe, step)


def kernel(x, cond_2048, L0_cond_W_ada, L0_cond_b_ada, L0_cond_Wq, L0_cond_Wkd, L0_cond_Wku, L0_cond_Wvu, L0_cond_Wo):
    import concourse.bacc as bacc
    from concourse.bass_utils import run_bass_kernel_spmd

    contig = np.ascontiguousarray
    by_tile = lambda w: contig(w.reshape(KT, P, -1).transpose(1, 0, 2))
    w_q, w_ku, w_vu, w_o = (np.asarray(w) for w in (L0_cond_Wq, L0_cond_Wku, L0_cond_Wvu, L0_cond_Wo))
    w_q_t = w_q.reshape(G, J, HD, D).transpose(3, 1, 0, 2).reshape(D, DQ)
    w_o_t = w_o.reshape(D, G, 2, 2, HD).transpose(2, 1, 4, 3, 0).reshape(P, 2, D)
    arrays = {
        "x": np.asarray(x).reshape(B * T, D),
        "cond_t": by_tile(np.asarray(cond_2048).T),
        "w_ada_t": by_tile(np.asarray(L0_cond_W_ada).T),
        "b_ada": contig(np.asarray(L0_cond_b_ada).reshape(2 * KT, P).T),
        "w_q_t": by_tile(w_q_t),
        "w_kd": np.asarray(L0_cond_Wkd),
        "w_kuv_t": contig(np.concatenate([w_ku.T, w_vu.T], axis=1)),
        "w_o_t": contig(w_o_t),
        "tables": rope_tables(),
        "ident": np.eye(P, dtype=np.float32),
    }
    nc = bacc.Bacc("TRN2", target_bir_lowering=False, num_devices=1)
    args = [nc.dram_tensor(n, a.shape, F32, kind="ExternalInput").ap() for n, a in arrays.items()]
    out = nc.dram_tensor("out", (B * T, D), F32, kind="ExternalOutput").ap()
    cond_attention_kernel(nc, *args, out)
    r = run_bass_kernel_spmd(nc, [arrays], core_ids=[0])
    return r.results[0]["out"].reshape(B, T, D)
```

```python
from contextlib import ExitStack

import numpy as np

import concourse.bass as bass
from concourse import mybir

F32 = mybir.dt.float32
F32R = mybir.dt.float32r
ALU = mybir.AluOpType
ACT = mybir.ActivationFunctionType
AX = mybir.AxisListType

P = 128
B, T, D = 128, 32, 256
HQ, G, HD = 16, 4, 16
J = HQ // G
HALF = HD // 2
LATENT = 64
EPS = 1e-5
THETA = 10000.0
SCALE = float(HD) ** -0.5
BU = P // T
UNITS = B * T // P
KT = D // P
GD = G * HD
DQ = HQ * HD
LOAD_AHEAD = 14
V_BUFFERS = 4

BODY = 8
FIRST_FULL = 8
LAST_FULL = (UNITS - 5) // BODY * BODY
FIRST, LAST = -5, UNITS + 4


def rope_tables():
    freqs = (1.0 / np.float32(THETA) ** (np.arange(0, HD, 2, dtype=np.float32) / np.float32(HD))).astype(np.float32)
    emb = np.arange(T, dtype=np.float32)[:, None] * freqs[None, :]
    cos, sin = np.cos(emb).astype(np.float32), np.sin(emb).astype(np.float32)
    halves = lambda first, second: np.concatenate([first, second], 1)
    plain = np.stack([halves(cos, cos), halves(sin, sin)], 1)
    swap = np.stack([halves(-sin, sin), halves(cos, -cos)], 1)
    return np.tile(np.stack([plain, swap], 1), (BU, 1, 1, 1)).astype(np.float32)


def cond_attention_kernel(nc, x, ada_t, w_q_t, w_kv, w_o_t, consts, out):
    x_units = x.rearrange("(u p) d -> u p d", p=P)
    out_units = out.rearrange("(u p) d -> u p d", p=P)

    with ExitStack() as ctx:
        def sb(name, shape, dtype=F32):
            return ctx.enter_context(nc.sbuf_tensor(name, shape, dtype))

        def bank(name):
            return ctx.enter_context(nc.psum_tensor(name, [P, 512], F32))

        def sem(name):
            return ctx.enter_context(nc.semaphore(name))

        const_in_sb = sb("const_in_sb", [P, P + 2 * 2 * HD + 2 * KT])
        ident_sb = const_in_sb[:, 0:P]
        tab_sb = const_in_sb[:, P:P + 2 * 2 * HD].rearrange("p (m s c) -> p m s c", m=2, s=2)
        b_ada_sb = const_in_sb[:, P + 2 * 2 * HD:]
        ada_sb = sb("ada_sb", [P, KT, 2 * D + B])
        w_kv_sb = sb("w_kv_sb", [LATENT, D + 2 * GD])
        w_qkv_sb = sb("w_qkv_sb", [P, KT, DQ + 2 * GD])
        w_hi_sb = sb("w_hi_sb", [P, KT, DQ + 2 * GD], F32R)
        w_lo_sb = sb("w_lo_sb", [P, KT, DQ + 2 * GD], F32R)
        w_o_sb = sb("w_o_sb", [P, 2, D])
        w_o_hi_sb = sb("w_o_hi_sb", [P, 2, D], F32R)
        w_o_lo_sb = sb("w_o_lo_sb", [P, 2, D], F32R)
        scale1_sb = sb("scale1_sb", [P, KT, B])
        shift_sb = sb("shift_sb", [P, KT, B])
        x_sb = sb("x_sb", [P, UNITS, D])
        warm_sb = sb("warm_sb", [P, P])
        bn_sb = sb("bn_sb", [P, 2, 6])
        mv_sb = sb("mv_sb", [P, 2, 2])
        veps_sb = sb("veps_sb", [P, 2, 1])
        const_sb = sb("const_sb", [P, 2])
        rstd_sb = sb("rstd_sb", [P, 2, 1])
        xhat_sb = sb("xhat_sb", [P, 2, D])
        h_sb = sb("h_sb", [P, 2, KT, P])
        h_hi_sb = sb("h_hi_sb", [P, 2, KT, P], F32R)
        h_lo_sb = sb("h_lo_sb", [P, 2, KT, P], F32R)
        q_rope_sb = sb("q_rope_sb", [P, 2, J * G, 2, HD])
        k_sb = sb("k_sb", [P, 2, GD])
        k_rope_sb = sb("k_rope_sb", [P, 2, G, 2, HD])
        k_swap_sb = sb("k_swap_sb", [P, 2, G, 2, HD])
        q_t_sb = sb("q_t_sb", [P, 2, BU, J, T])
        k_bd_sb = sb("k_bd_sb", [P, 2, BU, G, T])
        v_bd_sb = sb("v_bd_sb", [P, V_BUFFERS, BU, G, HD])
        prob_sb = sb("prob_sb", [P, 2, BU * G, T])
        max_sb = sb("max_sb", [P, 2, BU * G])
        sum_sb = sb("sum_sb", [P, 2, BU * G])
        inv_sb = sb("inv_sb", [P, 2, BU * G])
        prob_t_sb = sb("prob_t_sb", [P, 2, BU, P])
        y_sb = sb("y_sb", [P, 2, 2, BU, T])
        y_hi_sb = sb("y_hi_sb", [P, 2, 2, BU, T], F32R)
        y_lo_sb = sb("y_lo_sb", [P, 2, 2, BU, T], F32R)

        xt_ps = bank("xt_ps")
        qkv_ps = bank("qkv_ps")
        qt_ps = bank("qt_ps")
        kt_ps = bank("kt_ps")
        s_ps = bank("s_ps")
        pt_ps = bank("pt_ps")
        yt_ps = bank("yt_ps")
        o_ps = bank("o_ps")

        const_in, ada_in, kv_in, w_q_in, w_o_in = (sem(n) for n in ("const_in", "ada_in", "kv_in", "w_q_in", "w_o_in"))
        const_ready = sem("const_ready")
        warm_ready = sem("warm_ready")
        zeroed = sem("zeroed")
        ada_done = sem("ada_done")
        scale_ready = sem("scale_ready")
        shift_ready = sem("shift_ready")
        kv_done = sem("kv_done")
        w_ready = sem("w_ready")
        w_hi_done = sem("w_hi_done")
        w_lo_done = sem("w_lo_done")
        w_o_hi_done = sem("w_o_hi_done")
        w_o_lo_done = sem("w_o_lo_done")
        x_in = [sem("x_in_even"), sem("x_in_odd")]
        bn_done = sem("bn_done")
        stats_done = sem("stats_done")
        veps_done = sem("veps_done")
        rstd_done = sem("rstd_done")
        norm_done = sem("norm_done")
        xt_done = sem("xt_done")
        mod_done = sem("mod_done")
        h_done = sem("h_done")
        h_hi_done = sem("h_hi_done")
        h_lo_done = sem("h_lo_done")
        qkv_done = sem("qkv_done")
        rope_done = sem("rope_done")
        k_read = sem("k_read")
        k_parts_done = sem("k_parts_done")
        k_rope_done = sem("k_rope_done")
        qt_done = sem("qt_done")
        kt_done = sem("kt_done")
        qt_read = sem("qt_read")
        k_bd_done = sem("k_bd_done")
        v_bd_done = sem("v_bd_done")
        s_done = sem("s_done")
        max_done = sem("max_done")
        sub_done = sem("sub_done")
        exp_done = sem("exp_done")
        sum_done = sem("sum_done")
        inv_done = sem("inv_done")
        prob_done = sem("prob_done")
        pt_done = sem("pt_done")
        pt_read = sem("pt_read")
        yt_done = sem("yt_done")
        yt_read = sem("yt_read")
        y_hi_done = sem("y_hi_done")
        y_lo_done = sem("y_lo_done")
        o_done = sem("o_done")
        res_done = sem("res_done")
        stored = sem("stored")

        def has(u):
            return not isinstance(u, int) or 0 <= u < UNITS

        def later(u, n):
            return not isinstance(u, int) or u >= n

        def steps(eng, step):
            for i in range(FIRST, FIRST_FULL):
                step(i, i % BODY)
            with eng.Fori(FIRST_FULL // BODY, LAST_FULL // BODY) as four:
                for s in range(BODY):
                    step(four * BODY + s, s)
            for i in range(LAST_FULL, LAST):
                step(i, i % BODY)

        def at(stage, i, s, ahead):
            if has(i + ahead):
                stage(i + ahead, (s + ahead) % BODY)

        block = ctx.enter_context(nc.Block())

        @block.sync
        def _(sp):
            def load(u, p):
                if later(u, 2):
                    sp.wait_ge(x_in[p], 8 * (u - p))
                sp.dma_start(x_sb[:, bass.ds(u, 1), :], x_units[bass.ds(u, 1)].rearrange("u p d -> p u d")).then_inc(x_in[p], 16)

            def store(u):
                sp.wait_ge(res_done, u + 1)
                sp.dma_start(out_units[bass.ds(u, 1)].rearrange("u p d -> p u d"), x_sb[:, bass.ds(u, 1), :]).then_inc(stored, 16)

            load(0, 0)
            sp.dma_start(w_kv_sb[:], w_kv).then_inc(kv_in, 16)
            sp.dma_start(w_qkv_sb[:, :, 0:DQ], w_q_t).then_inc(w_q_in, 16)
            load(1, 1)
            for u in range(2, LOAD_AHEAD):
                load(u, u % 2)
                if u == 4:
                    sp.dma_start(w_o_sb[:], w_o_t).then_inc(w_o_in, 16)
            with sp.Fori(0, (UNITS - LOAD_AHEAD) // 2) as pair:
                for p in range(2):
                    load(pair * 2 + (LOAD_AHEAD + p), p)
                    store(pair * 2 + p)
            with sp.Fori(UNITS - LOAD_AHEAD, UNITS) as u:
                store(u)
            sp.wait_ge(stored, 16 * UNITS)

        @block.gpsimd
        def _(pool):
            pool.memset(const_sb[:, 0:1], EPS).then_inc(const_ready, 1)
            pool.memset(const_sb[:, 1:2], -0.5).then_inc(const_ready, 1)
            pool.memset(v_bd_sb[:], 0.0).then_inc(zeroed, 1)
            pool.memset(k_bd_sb[:], 0.0).then_inc(zeroed, 1)
            pool.wait_ge(const_ready, 2)

            def rstd(u, n):
                p = n % 2
                pool.wait_ge(stats_done, u + 1)
                if later(u, 2):
                    pool.wait_ge(norm_done, u - 1)
                pool.tensor_tensor(veps_sb[:, p], mv_sb[:, p, 1:2], const_sb[:, 0:1], ALU.add).then_inc(veps_done, 1)
                pool.wait_ge(veps_done, u + 1)
                pool.tensor_tensor(rstd_sb[:, p], veps_sb[:, p], const_sb[:, 1:2], ALU.pow).then_inc(rstd_done, 1)

            def weights_low():
                pool.wait_ge(w_o_hi_done, 1)
                pool.tensor_tensor(w_o_lo_sb[:], w_o_sb[:], w_o_hi_sb[:].bitcast(F32), ALU.subtract).then_inc(w_o_lo_done, 1)

            def shift(u, n):
                p = n % 2
                if isinstance(u, int) and u == 0:
                    pool.wait_ge(shift_ready, KT)
                pool.wait_ge(mod_done, u + 1)
                pool.tensor_tensor(
                    h_sb[:, p].rearrange("c k (b t) -> c k b t", b=BU),
                    h_sb[:, p].rearrange("c k (b t) -> c k b t", b=BU),
                    shift_sb[:, :, bass.ds(u * BU, BU)].unsqueeze(3).broadcast_to([P, KT, BU, T]),
                    ALU.add,
                ).then_inc(h_done, 1)

            def k_rope(u, n):
                p = n % 2
                if isinstance(u, int) and u == 0:
                    pool.wait_ge(const_in, 16)
                pool.wait_ge(k_read, u + 1)
                if later(u, 2):
                    pool.wait_ge(kt_done, u - 1)
                k = k_sb[:, p].rearrange("p (g h i) -> p g h i", g=G, h=2)
                pool.tensor_tensor(
                    k_rope_sb[:, p].rearrange("p g s c -> p s g c"),
                    k_sb[:, p].rearrange("p (g c) -> p g c", g=G).unsqueeze(1).broadcast_to([P, 2, G, HD]),
                    tab_sb[:, 0].unsqueeze(2).broadcast_to([P, 2, G, HD]), ALU.mult,
                ).then_inc(k_parts_done, 1)
                for half in range(2):
                    here = slice(half * HALF, (half + 1) * HALF)
                    pool.tensor_tensor(
                        k_swap_sb[:, p, :, :, here].rearrange("p g s i -> p s g i"),
                        k[:, :, 1 - half].unsqueeze(1).broadcast_to([P, 2, G, HALF]),
                        tab_sb[:, 1, :, here].unsqueeze(2).broadcast_to([P, 2, G, HALF]), ALU.mult,
                    ).then_inc(k_parts_done, 1)
                pool.wait_ge(k_parts_done, 3 * (u + 1))
                pool.tensor_tensor(k_rope_sb[:, p], k_rope_sb[:, p], k_swap_sb[:, p], ALU.add).then_inc(k_rope_done, 1)

            def divide(u, n):
                p = n % 2
                pool.wait_ge(inv_done, u + 1)
                pool.tensor_tensor(
                    prob_sb[:, p], prob_sb[:, p],
                    inv_sb[:, p].unsqueeze(2).broadcast_to([P, BU * G, T]), ALU.mult,
                ).then_inc(prob_done, 1)

            def y_low(u, n):
                p = n % 2
                pool.wait_ge(y_hi_done, u + 1)
                if later(u, 2):
                    pool.wait_ge(o_done, u - 1)
                pool.tensor_tensor(y_lo_sb[:, p], y_sb[:, p], y_hi_sb[:, p].bitcast(F32), ALU.subtract).then_inc(y_lo_done, 1)

            def step(i, s):
                at(k_rope, i, s, 0)
                at(rstd, i, s, 4)
                at(shift, i, s, 2)
                at(y_low, i, s, -3)
                at(divide, i, s, -1)
                if isinstance(i, int) and i == 1:
                    weights_low()

            steps(pool, step)

        @block.vector
        def _(dve):
            dve.memset(warm_sb[:], 0.0).then_inc(warm_ready, 1)

            def stats(u, n):
                p = n % 2
                dve.wait_ge(x_in[p], 8 * (u - p) + 16)
                dve.bn_stats(bn_sb[:, p], x_sb[:, bass.ds(u, 1), :].rearrange("p u d -> p (u d)")).then_inc(bn_done, 1)
                dve.wait_ge(bn_done, u + 1)

            def stats_sum(u, n):
                p = n % 2
                dve.bn_aggr(mv_sb[:, p], bn_sb[:, p]).then_inc(stats_done, 1)

            def norm(u, n):
                p = n % 2
                dve.wait_ge(rstd_done, u + 1)
                if later(u, 2):
                    dve.wait_ge(xt_done, u - 1)
                dve.tensor_scalar(
                    xhat_sb[:, p], x_sb[:, bass.ds(u, 1), :].rearrange("p u d -> p (u d)"),
                    mv_sb[:, p, 0:1], rstd_sb[:, p], ALU.subtract, ALU.mult,
                ).then_inc(norm_done, 1)

            def mod(u, n):
                p = n % 2
                dve.wait_ge(xt_done, u + 1)
                if later(u, 2):
                    dve.wait_ge(h_lo_done, u - 1)
                dve.tensor_tensor(
                    h_sb[:, p].rearrange("c k (b t) -> c k b t", b=BU),
                    xt_ps[:, 0:D].rearrange("c (k b t) -> c k b t", k=KT, b=BU),
                    scale1_sb[:, :, bass.ds(u * BU, BU)].unsqueeze(3).broadcast_to([P, KT, BU, T]),
                    ALU.mult,
                ).then_inc(mod_done, 1)

            def rope(u, n):
                p = n % 2
                dve.wait_ge(qkv_done, u + 1)
                if later(u, 2):
                    dve.wait_ge(qt_done, u - 1)
                dve.tensor_tensor(
                    q_rope_sb[:, p].rearrange("p r s c -> p s r c"),
                    qkv_ps[:, 0:DQ].rearrange("p (r c) -> p r c", c=HD).unsqueeze(1).broadcast_to([P, 2, J * G, HD]),
                    tab_sb[:, 0].unsqueeze(2).broadcast_to([P, 2, J * G, HD]), ALU.mult,
                ).then_inc(rope_done, 1)

            scores = s_ps[:, :].rearrange("p (r s) -> p r s", s=T)

            def row_max(u, n):
                p = n % 2
                dve.wait_ge(s_done, u + 1)
                dve.tensor_reduce(max_sb[:, p], scores, AX.X, ALU.max).then_inc(max_done, 1)

            def subtract_max(u, n):
                p = n % 2
                dve.wait_ge(max_done, u + 1)
                if later(u, 2):
                    dve.wait_ge(pt_done, u - 1)
                dve.tensor_tensor(
                    prob_sb[:, p], scores, max_sb[:, p].unsqueeze(2).broadcast_to([P, BU * G, T]), ALU.subtract,
                ).then_inc(sub_done, 1)

            def row_sum(u, n):
                p = n % 2
                dve.wait_ge(exp_done, u + 1)
                dve.tensor_reduce(sum_sb[:, p], prob_sb[:, p], AX.X, ALU.add).then_inc(sum_done, 1)

            def inverse(u, n):
                p = n % 2
                dve.wait_ge(sum_done, u + 1)
                dve.reciprocal(inv_sb[:, p], sum_sb[:, p]).then_inc(inv_done, 1)

            def h_low(u, n):
                p = n % 2
                dve.wait_ge(h_hi_done, u + 1)
                if later(u, 2):
                    dve.wait_ge(qkv_done, u - 1)
                dve.tensor_tensor(h_lo_sb[:, p], h_sb[:, p], h_hi_sb[:, p].bitcast(F32), ALU.subtract).then_inc(h_lo_done, 1)

            def residual(u, n):
                dve.wait_ge(o_done, u + 1)
                row = x_sb[:, bass.ds(u, 1), :].rearrange("p u d -> p (u d)")
                dve.tensor_tensor(row, o_ps[:, 0:D], row, ALU.add).then_inc(res_done, 1)

            def scale():
                dve.wait_ge(const_in, 16)
                dve.wait_ge(ada_done, 1)
                for k in range(KT):
                    dve.tensor_scalar(scale1_sb[:, k], s_ps[:, k * P:(k + 1) * P], b_ada_sb[:, k:k + 1], 1.0,
                                      ALU.add, ALU.add).then_inc(scale_ready, 1)
                dve.wait_ge(scale_ready, KT)

            def weights_low():
                dve.wait_ge(w_hi_done, 1)
                dve.tensor_tensor(w_lo_sb[:], w_qkv_sb[:], w_hi_sb[:].bitcast(F32), ALU.subtract).then_inc(w_lo_done, 1)

            def step(i, s):
                at(norm, i, s, 3)
                if isinstance(i, int) and i == -2:
                    scale()
                at(mod, i, s, 2)
                if isinstance(i, int) and i == -2:
                    weights_low()
                at(stats, i, s, 5)
                at(row_sum, i, s, -1)
                at(inverse, i, s, -1)
                at(rope, i, s, 1)
                at(residual, i, s, -4)
                at(h_low, i, s, 2)
                at(row_max, i, s, 0)
                at(stats_sum, i, s, 5)
                at(subtract_max, i, s, 0)

            steps(dve, step)

        @block.scalar
        def _(act):
            act.dma_start(ada_sb[:], ada_t).then_inc(ada_in, 16)
            act.dma_start(const_in_sb[:], consts).then_inc(const_in, 16)
            act.wait_ge(kv_done, 1)
            act.activation(w_qkv_sb[:, :, DQ:], pt_ps[:, 0:KT * 2 * GD].rearrange("p (k n) -> p k n", k=KT),
                           ACT.Copy).then_inc(w_ready, 1)
            act.wait_ge(w_q_in, 16)
            act.wait_ge(w_ready, 1)
            act.activation(w_hi_sb[:], w_qkv_sb[:], ACT.Copy).then_inc(w_hi_done, 1)
            act.wait_ge(const_in, 16)
            act.wait_ge(ada_done, 2)
            for k in range(KT):
                act.activation(shift_sb[:, k], yt_ps[:, k * P:(k + 1) * P], ACT.Identity,
                               bias=b_ada_sb[:, KT + k:KT + k + 1]).then_inc(shift_ready, 1)
            act.wait_ge(zeroed, 2)

            def weights_high():
                act.wait_ge(w_o_in, 16)
                act.activation(w_o_hi_sb[:], w_o_sb[:], ACT.Copy).then_inc(w_o_hi_done, 1)

            def y_out(u, n):
                p = n % 2
                act.wait_ge(yt_done, u + 1)
                if later(u, 2):
                    act.wait_ge(y_lo_done, u - 1)
                heads = yt_ps[0:GD, :].rearrange("c (b j l t) -> c j l b t", b=BU, j=2, l=2)
                for half in range(2):
                    last = act.activation(y_sb[half * GD:(half + 1) * GD, p], heads[:, half], ACT.Copy)
                last.then_inc(yt_read, 1)

            def y_high(u, n):
                p = n % 2
                act.wait_ge(yt_read, u + 1)
                if later(u, 2):
                    act.wait_ge(o_done, u - 1)
                act.activation(y_hi_sb[:, p], y_sb[:, p], ACT.Copy).then_inc(y_hi_done, 1)

            def k_raw_out(u, n):
                p = n % 2
                act.wait_ge(rope_done, u + 1)
                if later(u, 2):
                    act.wait_ge(k_rope_done, u - 1)
                act.activation(k_sb[:, p], qkv_ps[:, DQ:DQ + GD], ACT.Copy).then_inc(k_read, 1)

            def v_out(u, n):
                if later(u, V_BUFFERS):
                    act.wait_ge(yt_done, u - (V_BUFFERS - 1))
                for b in range(BU):
                    for g in range(G):
                        c = DQ + GD + g * HD
                        last = act.activation(v_bd_sb[g * T:(g + 1) * T, n % V_BUFFERS, b, g], qkv_ps[b * T:(b + 1) * T, c:c + HD], ACT.Copy)
                last.then_inc(v_bd_done, 1)

            def h_high(u, n):
                p = n % 2
                act.wait_ge(h_done, u + 1)
                if later(u, 2):
                    act.wait_ge(qkv_done, u - 1)
                act.activation(h_hi_sb[:, p], h_sb[:, p], ACT.Copy).then_inc(h_hi_done, 1)

            def pt_out(u, n):
                p = n % 2
                act.wait_ge(pt_done, u + 1)
                if later(u, 2):
                    act.wait_ge(yt_done, u - 1)
                act.activation(prob_t_sb[:, p], pt_ps[:, :].rearrange("p (b q) -> p b q", b=BU), ACT.Copy).then_inc(pt_read, 1)

            def exps(u, n):
                p = n % 2
                act.wait_ge(sub_done, u + 1)
                act.activation(prob_sb[:, p], prob_sb[:, p], ACT.Exp, scale=SCALE).then_inc(exp_done, 1)

            def q_out(u, n):
                p = n % 2
                act.wait_ge(qt_done, u + 1)
                if later(u, 2):
                    act.wait_ge(s_done, u - 1)
                act.activation(q_t_sb[:, p].rearrange("c b j t -> c j b t"),
                               qt_ps[:, :].rearrange("c (j b t) -> c j b t", j=J, b=BU), ACT.Copy).then_inc(qt_read, 1)

            def k_out(u, n):
                p = n % 2
                act.wait_ge(kt_done, u + 1)
                if later(u, 2):
                    act.wait_ge(s_done, u - 1)
                for g in range(G):
                    rows = slice(g * P // G, (g + 1) * P // G)
                    last = act.activation(k_bd_sb[rows, p, :, g], kt_ps[rows, 0:P].rearrange("c (b t) -> c b t", b=BU), ACT.Copy)
                last.then_inc(k_bd_done, 1)

            def step(i, s):
                at(y_high, i, s, -3)
                at(pt_out, i, s, -2)
                at(exps, i, s, -1)
                if isinstance(i, int) and i == 1:
                    weights_high()
                at(q_out, i, s, 0)
                at(k_out, i, s, 0)
                at(h_high, i, s, 2)
                at(y_out, i, s, -2)
                at(k_raw_out, i, s, 1)
                at(v_out, i, s, 1)

            steps(act, step)

        @block.tensor
        def _(pe):
            def warm(products):
                for _ in range(products):
                    pe.matmul(o_ps[:, 0:P], warm_sb[:], warm_sb[:], start=True, stop=True)

            def modulation(part, ps):
                for m in range(KT):
                    row = part * D + m * P
                    for k in range(KT):
                        last = pe.matmul(ps[:, m * P:(m + 1) * P], ada_sb[:, k, row:row + P], ada_sb[:, k, 2 * D:],
                                         start=(k == 0), stop=(k == KT - 1))
                last.then_inc(ada_done, 1)

            pe.wait_ge(warm_ready, 1)
            warm(10)
            pe.wait_ge(ada_in, 16)
            modulation(0, s_ps)
            pe.wait_ge(kv_in, 16)
            for k in range(KT):
                last = pe.matmul(pt_ps[:, k * 2 * GD:(k + 1) * 2 * GD], w_kv_sb[:, k * P:(k + 1) * P], w_kv_sb[:, D:],
                                 start=True, stop=True)
            last.then_inc(kv_done, 1)
            modulation(1, yt_ps)
            pe.wait_ge(const_in, 16)

            def qkv(u, n):
                p = n % 2
                if isinstance(u, int) and u == 0:
                    pe.wait_ge(w_lo_done, 1)
                pe.wait_ge(h_hi_done, u + 1)
                if later(u, 1):
                    pe.wait_ge(v_bd_done, u)
                for h, w in ((h_hi_sb, w_lo_sb), (h_lo_sb, w_hi_sb), (h_hi_sb, w_hi_sb)):
                    if h is h_lo_sb:
                        pe.wait_ge(h_lo_done, u + 1)
                    for k in range(KT):
                        last = pe.matmul(qkv_ps[:, 0:DQ + 2 * GD], h[:, p, k], w[:, k],
                                         start=(w is w_lo_sb and k == 0), stop=(w is w_hi_sb and h is h_hi_sb and k == KT - 1))
                last.then_inc(qkv_done, 1)

            def scores(u, n):
                p = n % 2
                pe.wait_ge(qt_read, u + 1)
                pe.wait_ge(k_bd_done, u + 1)
                if later(u, 1):
                    pe.wait_ge(sub_done, u)
                else:
                    pe.wait_ge(scale_ready, KT)
                for b in range(BU):
                    last = pe.matmul(s_ps[:, b * P:(b + 1) * P], q_t_sb[:, p, b].rearrange("c j t -> c (j t)"),
                                     k_bd_sb[:, p, b].rearrange("c g t -> c (g t)"), start=True, stop=True)
                last.then_inc(s_done, 1)

            def prob_t(u, n):
                p = n % 2
                pe.wait_ge(prob_done, u + 1)
                if later(u, 1):
                    pe.wait_ge(pt_read, u)
                else:
                    pe.wait_ge(w_ready, 1)
                for b in range(BU):
                    last = pe.transpose(pt_ps[:, b * P:(b + 1) * P],
                                        prob_sb[:, p, b * G:(b + 1) * G].rearrange("p g t -> p (g t)"), ident_sb)
                last.then_inc(pt_done, 1)

            def xhat_t(u, n):
                p = n % 2
                pe.wait_ge(norm_done, u + 1)
                if later(u, 1):
                    pe.wait_ge(mod_done, u)
                for k in range(KT):
                    last = pe.transpose(xt_ps[:, k * P:(k + 1) * P], xhat_sb[:, p, k * P:(k + 1) * P], ident_sb)
                last.then_inc(xt_done, 1)

            def project(u, n):
                p = n % 2
                pe.wait_ge(y_lo_done, u + 1)
                if later(u, 1):
                    pe.wait_ge(res_done, u)
                else:
                    pe.wait_ge(w_o_lo_done, 1)
                for y, w in ((y_hi_sb, w_o_lo_sb), (y_lo_sb, w_o_hi_sb), (y_hi_sb, w_o_hi_sb)):
                    for l in range(2):
                        last = pe.matmul(o_ps[:, 0:D], y[:, p, l].rearrange("c b t -> c (b t)"), w[:, l],
                                         start=(w is w_o_lo_sb and l == 0), stop=(w is w_o_hi_sb and y is y_hi_sb and l == 1))
                last.then_inc(o_done, 1)

            def q_t(u, n):
                p = n % 2
                pe.wait_ge(rope_done, u + 1)
                if later(u, 1):
                    pe.wait_ge(qt_read, u)
                for j in range(J):
                    last = pe.transpose(qt_ps[:, j * P:(j + 1) * P], q_rope_sb[:, p, j * G:(j + 1) * G].rearrange("p g s c -> p (g s c)"), ident_sb)
                last.then_inc(qt_done, 1)

            def k_t(u, n):
                p = n % 2
                pe.wait_ge(k_rope_done, u + 1)
                if later(u, 1):
                    pe.wait_ge(k_bd_done, u)
                pe.transpose(kt_ps[:, 0:P], k_rope_sb[:, p].rearrange("p g s c -> p (g s c)"), ident_sb).then_inc(kt_done, 1)

            def heads_out(u, n):
                p = n % 2
                pe.wait_ge(pt_read, u + 1)
                pe.wait_ge(v_bd_done, u + 1)
                if later(u, 1):
                    pe.wait_ge(yt_read, u)
                else:
                    pe.wait_ge(shift_ready, KT)
                for b in range(BU):
                    last = pe.matmul(yt_ps[0:GD, b * P:(b + 1) * P], v_bd_sb[:, n % V_BUFFERS, b].rearrange("c g d -> c (g d)"),
                                     prob_t_sb[:, p, b], start=True, stop=True)
                last.then_inc(yt_done, 1)

            def step(i, s):
                if isinstance(i, int) and -2 <= i < 1:
                    warm(2 if i < -1 else 2)
                at(qkv, i, s, 1)
                at(k_t, i, s, 0)
                at(xhat_t, i, s, 3)
                at(heads_out, i, s, -2)
                at(scores, i, s, 0)
                at(q_t, i, s, 1)
                at(prob_t, i, s, -1)
                at(project, i, s, -3)

            steps(pe, step)


def kernel(x, cond_2048, L0_cond_W_ada, L0_cond_b_ada, L0_cond_Wq, L0_cond_Wkd, L0_cond_Wku, L0_cond_Wvu, L0_cond_Wo):
    import concourse.bacc as bacc
    from concourse.bass_utils import run_bass_kernel_spmd

    contig = np.ascontiguousarray
    by_tile = lambda w: contig(w.reshape(KT, P, -1).transpose(1, 0, 2))
    w_q, w_ku, w_vu, w_o = (np.asarray(w) for w in (L0_cond_Wq, L0_cond_Wku, L0_cond_Wvu, L0_cond_Wo))
    w_q_t = w_q.reshape(G, J, HD, D).transpose(3, 1, 0, 2).reshape(D, DQ)
    w_o_t = w_o.reshape(D, G, 2, 2, HD).transpose(2, 1, 4, 3, 0).reshape(P, 2, D)
    arrays = {
        "x": np.asarray(x).reshape(B * T, D),
        "ada_t": by_tile(np.concatenate([np.asarray(L0_cond_W_ada).T, np.asarray(cond_2048).T], axis=1)),
        "w_q_t": by_tile(w_q_t),
        "w_kv": contig(np.concatenate([np.asarray(L0_cond_Wkd), w_ku.T, w_vu.T], axis=1)),
        "w_o_t": contig(w_o_t),
        "consts": np.concatenate([np.eye(P, dtype=np.float32), rope_tables().reshape(P, -1),
                                  np.asarray(L0_cond_b_ada).reshape(2 * KT, P).T], axis=1),
    }
    nc = bacc.Bacc("TRN2", target_bir_lowering=False, num_devices=1)
    args = [nc.dram_tensor(n, a.shape, F32, kind="ExternalInput").ap() for n, a in arrays.items()]
    out = nc.dram_tensor("out", (B * T, D), F32, kind="ExternalOutput").ap()
    cond_attention_kernel(nc, *args, out)
    r = run_bass_kernel_spmd(nc, [arrays], core_ids=[0])
    return r.results[0]["out"].reshape(B, T, D)
```
